# Optimizing a Trainium2 kernel written in Bass

```python
import numpy as np
import jax
import jax.numpy as jnp

def _softmax(x, axis=-1):
    return jax.nn.softmax(x, axis=axis)
def _gelu(x):
    return jax.nn.gelu(x, approximate=True)
def _silu(x):
    return jax.nn.silu(x)
def _sigmoid(x):
    return jax.nn.sigmoid(x)
def _layernorm(x, axis=-1, eps=1e-5):
    m = jnp.mean(x, axis=axis, keepdims=True)
    v = jnp.var(x, axis=axis, keepdims=True)
    return (x - m) / jnp.sqrt(v + eps)
def _scatter_add(tgt, idx, src, axis=0):
    return tgt.at[idx].add(src)
def _segment_sum(src, seg, n):
    return jax.ops.segment_sum(src, seg, n)

kernel_name = 'mk_conv_seq_d1_conv_nchw64_2396ea'

def setup_inputs(seed: int = 0):
    np.random.seed(seed)
    _w = jnp.asarray
    def _rec_inputs():
        import jax
        import jax.numpy as jnp
        _gk = jax.random.key(seed)
        x = 127.5 + 73.61 * jax.random.normal(jax.random.fold_in(_gk, 1), (16, 64, 256, 256), jnp.float32)
        return x
    x = _rec_inputs()
    def _L0_conv_setup():
        import jax, jax.numpy as jnp
        import numpy as np
        NUM_BINS = 256
        BN_EPS = 1e-05

        def _histc_argmax(x):
            B, C, H, W = x.shape
            flat = x.reshape(B * C, H * W)
            in_range = (flat >= 0.0) & (flat <= 255.0)
            idx = jnp.clip((flat * (NUM_BINS / 255.0)).astype(jnp.int32), 0, NUM_BINS - 1)
            rows = jnp.arange(B * C)[:, None]
            hist = jnp.zeros((B * C, NUM_BINS), dtype=jnp.float32).at[rows, idx].add(in_range.astype(jnp.float32))
            return hist.argmax(axis=-1).reshape(B, C)

        def _bn(a, gamma, beta, mean, var):
            inv = gamma * jax.lax.rsqrt(var + BN_EPS)
            return a * inv[None, :, None, None] + (beta - mean * inv)[None, :, None, None]
        key = jax.random.key(seed)
        ks = jax.random.split(key, 16)
        B, C, H, W = (16, 64, 256, 256)
        x = jax.random.uniform(ks[0], (B, C, H, W), dtype=jnp.float32) * 255.0
        return {'x': x, 'conv1_w': jax.random.normal(ks[1], (C, C), dtype=jnp.float32) * 0.05, 'conv1_b': jax.random.normal(ks[2], (C,), dtype=jnp.float32) * 0.05, 'bn1_gamma': jax.random.uniform(ks[3], (C,), dtype=jnp.float32) + 0.5, 'bn1_beta': jax.random.normal(ks[4], (C,), dtype=jnp.float32) * 0.05, 'bn1_mean': jax.random.normal(ks[5], (C,), dtype=jnp.float32) * 0.05, 'bn1_var': jax.random.uniform(ks[6], (C,), dtype=jnp.float32) + 0.5, 'conv2_w': jax.random.normal(ks[7], (1, C), dtype=jnp.float32) * 0.05, 'conv2_b': jax.random.normal(ks[8], (1,), dtype=jnp.float32) * 0.05, 'bn2_gamma': jax.random.uniform(ks[9], (1,), dtype=jnp.float32) + 0.5, 'bn2_beta': jax.random.normal(ks[10], (1,), dtype=jnp.float32) * 0.05, 'bn2_mean': jax.random.normal(ks[11], (1,), dtype=jnp.float32) * 0.05, 'bn2_var': jax.random.uniform(ks[12], (1,), dtype=jnp.float32) + 0.5}
    _L0_conv_all = _L0_conv_setup()
    _L0_conv_in = {k: v for k, v in _L0_conv_all.items() if k in ('conv1_w', 'conv1_b', 'bn1_gamma', 'bn1_beta', 'bn1_mean', 'bn1_var', 'conv2_w', 'conv2_b', 'bn2_gamma', 'bn2_beta', 'bn2_mean', 'bn2_var', )}
    del _L0_conv_all

    return {
        "x": x,
        "L0_conv_conv1_w": _L0_conv_in["conv1_w"],
        "L0_conv_conv1_b": _L0_conv_in["conv1_b"],
        "L0_conv_bn1_gamma": _L0_conv_in["bn1_gamma"],
        "L0_conv_bn1_beta": _L0_conv_in["bn1_beta"],
        "L0_conv_bn1_mean": _L0_conv_in["bn1_mean"],
        "L0_conv_bn1_var": _L0_conv_in["bn1_var"],
        "L0_conv_conv2_w": _L0_conv_in["conv2_w"],
        "L0_conv_conv2_b": _L0_conv_in["conv2_b"],
        "L0_conv_bn2_gamma": _L0_conv_in["bn2_gamma"],
        "L0_conv_bn2_beta": _L0_conv_in["bn2_beta"],
        "L0_conv_bn2_mean": _L0_conv_in["bn2_mean"],
        "L0_conv_bn2_var": _L0_conv_in["bn2_var"],
    }

def reference(x, L0_conv_conv1_w, L0_conv_conv1_b, L0_conv_bn1_gamma, L0_conv_bn1_beta, L0_conv_bn1_mean, L0_conv_bn1_var, L0_conv_conv2_w, L0_conv_conv2_b, L0_conv_bn2_gamma, L0_conv_bn2_beta, L0_conv_bn2_mean, L0_conv_bn2_var):
    import jax
    import jax.numpy as jnp
    def _L0_conv_ref(x, conv1_w, conv1_b, bn1_gamma, bn1_beta, bn1_mean, bn1_var, conv2_w, conv2_b, bn2_gamma, bn2_beta, bn2_mean, bn2_var):
        import jax, jax.numpy as jnp
        import numpy as np
        NUM_BINS = 256
        BN_EPS = 1e-05

        def _histc_argmax(x):
            B, C, H, W = x.shape
            flat = x.reshape(B * C, H * W)
            in_range = (flat >= 0.0) & (flat <= 255.0)
            idx = jnp.clip((flat * (NUM_BINS / 255.0)).astype(jnp.int32), 0, NUM_BINS - 1)
            rows = jnp.arange(B * C)[:, None]
            hist = jnp.zeros((B * C, NUM_BINS), dtype=jnp.float32).at[rows, idx].add(in_range.astype(jnp.float32))
            return hist.argmax(axis=-1).reshape(B, C)

        def _bn(a, gamma, beta, mean, var):
            inv = gamma * jax.lax.rsqrt(var + BN_EPS)
            return a * inv[None, :, None, None] + (beta - mean * inv)[None, :, None, None]
        bin_size = 256 // NUM_BINS
        dominant = _histc_argmax(x)
        pixel_bins = jnp.floor(x / bin_size).astype(jnp.int32)
        att = (pixel_bins != dominant[:, :, None, None]).astype(x.dtype)
        a = jnp.einsum('bchw,oc->bohw', att, conv1_w) + conv1_b[None, :, None, None]
        a = jax.nn.relu(_bn(a, bn1_gamma, bn1_beta, bn1_mean, bn1_var))
        a = jnp.einsum('bchw,oc->bohw', a, conv2_w) + conv2_b[None, :, None, None]
        a = jax.nn.sigmoid(_bn(a, bn2_gamma, bn2_beta, bn2_mean, bn2_var))
        return x * a

    def _gn(v, G=32, eps=1e-5):
        B_, C_, H_, W_ = v.shape
        g = v.reshape(B_, G, C_ // G, H_, W_)
        m = jnp.mean(g, axis=(2, 3, 4), keepdims=True)
        s = jnp.var(g, axis=(2, 3, 4), keepdims=True)
        return ((g - m) / jnp.sqrt(s + eps)).reshape(v.shape)

    def _ln_c(v, eps=1e-6):
        m = jnp.mean(v, axis=1, keepdims=True)
        s = jnp.var(v, axis=1, keepdims=True)
        return (v - m) / jnp.sqrt(s + eps)

    def _ln_t(v, eps=1e-5):
        m = jnp.mean(v, axis=-1, keepdims=True)
        s = jnp.var(v, axis=-1, keepdims=True)
        return (v - m) / jnp.sqrt(s + eps)

    def _to_tokens(v):
        B_, C_, H_, W_ = v.shape
        return v.reshape(B_, C_, H_ * W_).transpose(0, 2, 1)
    def _from_tokens(t, like):
        B_, C_, H_, W_ = like.shape
        return t.transpose(0, 2, 1).reshape(B_, C_, H_, W_)

    x = _L0_conv_ref(x, L0_conv_conv1_w, L0_conv_conv1_b, L0_conv_bn1_gamma, L0_conv_bn1_beta, L0_conv_bn1_mean, L0_conv_bn1_var, L0_conv_conv2_w, L0_conv_conv2_b, L0_conv_bn2_gamma, L0_conv_bn2_beta, L0_conv_bn2_mean, L0_conv_bn2_var)
    return x


_drawn_inputs = setup_inputs


def setup_inputs(seed=0):
    import zlib

    import numpy as np

    out = dict(_drawn_inputs(seed))
    spreads = {}
    factors = {'L0_conv_conv1_b': 6.153,
     'L0_conv_bn1_gamma': 3.944,
     'L0_conv_bn1_beta': 8.0,
     'L0_conv_bn1_mean': 4.569,
     'L0_conv_bn1_var': 5.179}
    for name, (base, spread) in spreads.items():
        noise = np.random.default_rng([zlib.crc32(name.encode()), seed]).standard_normal(out[name].shape)
        drawn = base * np.exp(spread * noise) if base else spread * noise
        out[name] = jnp.asarray(drawn.astype(out[name].dtype))
    for name, factor in factors.items():
        out[name] = (out[name] * factor).astype(out[name].dtype)
    return out
```

```python
import concourse.bass as bass
from concourse import mybir
from contextlib import ExitStack

C = 64
PIX = 256 * 256
P = 128
GC = 8
COLS = 128
ROW = PIX // P
QUARTERS = ROW // COLS
STEPS = 8
OCTETS = 4
SUB = COLS // STEPS
SHIFT = OCTETS * STEPS + 4
PACK = 16
PARTS = COLS // PACK
NH = 8
LOWS = (0, 1, 4, 5)
NL = len(LOWS)
BN_EPS = 1e-5



class Octet:

    def __init__(self, o, rep, image=0):
        self.o, self.rep, self.image = o, rep, image

    def count(self, step, lag):
        return self.o * STEPS + (step - lag)

    def exists(self, step, lag, total):
        return 0 <= self.rep * STEPS + step - lag < total

    def at_least(self, step, lag, least):
        return self.rep * STEPS + step - lag >= least


def octets(eng, images, body):
    total = images * OCTETS
    body(Octet(0, 0))
    with eng.Fori(1, OCTETS) as q:
        body(Octet(q, 1))
    body(Octet(OCTETS, OCTETS, 1))
    body(Octet(OCTETS + 1, OCTETS + 1, 1))
    with eng.Fori(OCTETS + 2, 2 * OCTETS) as q:
        body(Octet(q, OCTETS + 2, 1))
    with eng.Fori(2, images) as n:
        body(Octet(n * OCTETS, 2 * OCTETS, n))
        with eng.Fori(1, OCTETS) as q:
            body(Octet(n * OCTETS + q, 2 * OCTETS + 1, n))
    body(Octet(total, total, images))
    with eng.Fori(total + 1, total + OCTETS) as q:
        body(Octet(q, total + 1))
    body(Octet(total + OCTETS, total + OCTETS))
    body(Octet(total + OCTETS + 1, total + OCTETS + 1))


def build(nc, x, w1t, w2b, par, ident_in, keys_in, pick_in, out, bin_scale):
    fp32, bf16, fp16 = mybir.dt.float32, mybir.dt.bfloat16, mybir.dt.float16
    fp8, u16, i16, i32 = mybir.dt.float8e5, mybir.dt.uint16, mybir.dt.int16, mybir.dt.int32
    ALU, ACT, AX = mybir.AluOpType, mybir.ActivationFunctionType, mybir.AxisListType
    ds = bass.ds

    images = x.shape[0] // C
    n1 = images * OCTETS * STEPS
    N = GC * COLS
    ctx = ExitStack()
    with ctx:
        def sb(name, shape, dt):
            return ctx.enter_context(nc.sbuf_tensor(name, shape, dt))

        def pb(name, shape, dt):
            return ctx.enter_context(nc.psum_tensor(name, shape, dt))

        def sem(name):
            return ctx.enter_context(nc.semaphore(name))

        x1 = [sb(f"x1_{g}", [P, GC, ROW], fp32) for g in range(2)]
        scaled = sb("scaled", [P, N], fp32)
        halves = [sb(f"halves{i}", [P, N], i16) for i in range(2)]
        inrange = [sb(f"inrange{i}", [P, N], bf16) for i in range(2)]
        clipped = sb("clipped", [P, N], i16)
        code = sb("code", [P, N], u16)
        high = sb("high", [P, N], u16)
        low = sb("low", [P, N], u16)
        onehot_h = [sb(f"onehot_h{i}", [P, N * NH], u16) for i in range(2)]
        onehot_l = [sb(f"onehot_l{i}", [P, N * NL], u16) for i in range(2)]
        WM, WN = 2 * NH * GC, 2 * NL * GC
        big_int = sb("big_int", [P, PARTS * WN], i16)
        big = sb("big", [P, PARTS * WN], fp16)
        small = sb("small", [P, PARTS * WN], fp16)
        key = sb("key", [P, 2, 2 * WN], fp32)
        best = sb("best", [P, 2 * OCTETS], fp32)
        kmax = sb("kmax", [GC, GC], fp32)
        kint = sb("kint", [GC, GC], i32)
        kbin = sb("kbin", [GC, GC], i32)
        kval = sb("kval", [GC, GC], fp32)
        spread = sb("spread", [P, GC], fp32)
        dom = sb("dom", [P, 1], fp32)
        pat_lo = sb("pat_lo", [P, 1], fp32)
        pat = sb("pat", [P, 1], fp32)
        x2 = sb("x2", [P, 2, C, COLS], fp32)
        halves2 = [sb(f"halves2_{i}", [P, C * SUB], i16) for i in range(2)]
        floors = [sb(f"floors{i}", [P, C * SUB], i16) for i in range(2)]
        att = sb("att", [P, C * SUB], bf16)
        hidden = sb("hidden", [P, C * SUB], fp32)
        gate = sb("gate", [P, COLS], fp32)
        product = [sb(f"product{i}", [P, C // 4, COLS], fp32) for i in range(2)]
        ident = sb("ident", [P, P], fp32)
        ident_bf = sb("ident_bf", [P, P], bf16)
        ident_hf = sb("ident_hf", [P, P], fp16)
        keys = sb("keys", [P, 2, 2 * WN], fp32)
        pick = sb("pick", [P, P + GC], fp32)
        w_rest = sb("w_rest", [P, P], fp32)
        w_part = [sb(f"w_part{i}", [P, P], bf16) for i in range(3)]
        w2 = sb("w2", [P, 2], fp32)
        params = sb("params", [P, 10], fp32)
        minus_half = sb("minus_half", [P, 1], fp32)
        norm = sb("norm", [P, 8], fp32)

        counts = [pb(f"counts{i}", [P, PARTS * WN], fp32) for i in range(2)]
        totals = pb("totals", [P, 2, 2, WN], fp32)
        turned = pb("turned", [P, C * SUB], bf16)
        pre = [pb(f"pre{i}", [P, 512], fp32) for i in range(2)]
        logit = pb("logit", [P, 512], fp32)
        decode = pb("decode", [P, 512], fp32)

        consts_in = sem("consts_in")
        x1_in = [sem(f"x1_in{g}") for g in range(2)]
        x2_in = [sem(f"x2_in{k}") for k in range(4)]
        stored = [sem(f"stored{i}") for i in range(2)]
        setup_dve = sem("setup_dve")
        setup_pool = sem("setup_pool")
        s_scaled, s_prep, s_codes = sem("scaled_done"), sem("prep_done"), sem("codes_done")
        s_onehots, s_hist = sem("onehots_ready"), sem("hist_done")
        s_bigint, s_big, s_small = sem("bigint_ready"), sem("big_ready"), sem("small_ready")
        s_totals, s_key, s_best = sem("totals_done"), sem("key_ready"), sem("best_ready")
        s_bestT, s_dec, s_spread, s_pat = sem("best_turned"), sem("bins_chain"), sem("bins_spread"), sem("pat_ready")
        hist_begun = sem("hist_begun")
        s_pat2 = sem("pat_chain")
        s_halves2, s_floors, s_turned = sem("halves2_ready"), sem("floors_ready"), sem("turned_done")
        s_att, s_conv1, s_hidden = sem("att_ready"), sem("conv1_done"), sem("hidden_ready")
        s_conv2, s_gate, s_product = sem("conv2_done"), sem("gate_ready"), sem("product_ready")

        block = ctx.enter_context(nc.Block())
        SETUP = 17
        KEY_STEP, TURN_STEP = 2, 2

        def slot(oc, step):
            return oc.o % 2 if step >= 4 else (oc.o + 1) % 2

        @block.sync
        def _(sp):
            for dst, src in ((ident, ident_in), (pick, pick_in), (w_rest, w1t), (w2, w2b), (params, par)):
                sp.dma_start(dst[:, :], src).then_inc(consts_in, 16)
            sp.dma_start(keys[:, :, :], keys_in.rearrange("p (a b) -> p a b", a=2)).then_inc(consts_in, 16)

            def chunk(t, c, k):
                rows = t[ds((c // QUARTERS) * C + C // 4 * k, C // 4), :].rearrange("c (p t) -> p c t", p=P)
                return rows[:, :, ds((c % QUARTERS) * COLS, COLS)]

            def body(oc):
                o = oc.o
                if oc.exists(0, 0, n1):
                    for g in range(2):
                        if oc.rep > 0:
                            sp.wait_ge(s_prep, o * STEPS - STEPS + 4 * (g + 1))
                        src = x[ds((o * 2 + g) * GC, GC), :].rearrange("c (p t) -> p c t", p=P)
                        sp.dma_start(x1[g][:, :, :], src).then_inc(x1_in[g], 16)
                for k in range(4):
                    ch = C // 4
                    if oc.rep >= OCTETS + 2:
                        c = o - (OCTETS + 2)
                        sp.wait_ge(s_product, c * 4 + (k + 1))
                        sp.dma_start(chunk(out, c, k), product[k % 2][:, :, :])\
                            .then_inc(stored[k % 2], 16)
                    if oc.rep >= OCTETS and oc.rep < (images + 1) * OCTETS:
                        c = o - OCTETS
                        sp.dma_start(x2[:, ds(o % 2, 1), ch * k:ch * (k + 1), :].rearrange("p a c t -> p (a c) t"),
                                     chunk(x, c, k)).then_inc(x2_in[k], 16)

            octets(sp, images, body)
            for i in range(2):
                sp.wait_ge(stored[i], 16 * 2 * images * QUARTERS)

        @block.gpsimd
        def _(pool):
            pool.wait_ge(setup_dve, 2)
            nc.gpsimd.tensor_tensor(norm[:, 2:4], norm[:, 0:2], norm[:, 6:8], ALU.pow).then_inc(setup_pool, 1)

        @block.scalar
        def _(act):
            A = nc.scalar

            def by_column(t):
                return t.rearrange("p c t -> p t c")

            def body(oc):
                o = oc.o
                for j in range(STEPS):
                    if oc.exists(j, 0, n1):
                        i, b = oc.count(j, 0), j % 2
                        if j % 4 == 0:
                            act.wait_ge(x1_in[j // 4], (o + 1) * 16)
                        if oc.at_least(j, 0, 2):
                            act.wait_ge(s_codes, (i - 2) * 6 + 2)
                        src = by_column(x1[j // 4][:, :, COLS * (j % 4):COLS * (j % 4 + 1)])
                        A.activation(inrange[b][:, :].rearrange("p (t c) -> p t c", c=GC), src, ACT.Sign,
                                     scale=-1.0, bias=255.0 + 2.0 ** -16)
                        if oc.at_least(j, 0, 1):
                            act.wait_ge(s_prep, i)
                        A.activation(scaled[:, :].rearrange("p (t c) -> p t c", c=GC), src, ACT.Copy,
                                     scale=2.0 * bin_scale).then_inc(s_scaled, 1)
                        act.wait_ge(s_scaled, i + 1)
                        A.activation(halves[b][:, :], scaled[:, :], ACT.Copy, bias=-0.5).then_inc(s_prep, 1)
                    if oc.exists(j, SHIFT + 3, n1):
                        e = oc.count(j, SHIFT + 3)
                        for h in range(2):
                            act.wait_ge(s_conv1, e * 2 + (h + 1))
                            if h == 0 and oc.at_least(j, SHIFT + 3, 1):
                                act.wait_ge(s_conv2, e)
                            A.activation(hidden[:, 512 * h:512 * (h + 1)], pre[h][:, :], ACT.Relu,
                                         scale=norm[:, 4:5], bias=norm[:, 0:1]).then_inc(s_hidden, 1)
                    if oc.exists(j, 2, n1):
                        i = oc.count(j, 2)
                        act.wait_ge(s_hist, i + 1)
                        if oc.at_least(j, 2, 1):
                            act.wait_ge(s_small, i)
                            act.wait_ge(s_totals, i)
                        A.activation(big_int[:, :], counts[j % 2][:, :], ACT.Copy, scale=0.25).then_inc(s_bigint, 1)
                        act.wait_ge(s_bigint, i + 1)
                        A.activation(big[:, :], big_int[:, :], ACT.Copy).then_inc(s_big, 1)
                    if j == 7 and oc.exists(0, (OCTETS + 1) * STEPS, n1):
                        c = o - (OCTETS + 1)
                        act.wait_ge(s_conv2, (c + 1) * STEPS)
                        if oc.rep > OCTETS + 1:
                            act.wait_ge(s_product, c * 4)
                        A.activation(gate[:, :], logit[:, 0:COLS], ACT.Sigmoid,
                                     scale=norm[:, 5:6], bias=norm[:, 1:2]).then_inc(s_gate, 1)
                    if oc.exists(j, SHIFT, n1):
                        e, s = oc.count(j, SHIFT), (j - SHIFT) % STEPS
                        if s == 0:
                            for k in range(4):
                                act.wait_ge(x2_in[k], (o - OCTETS + 1) * 16)
                        if oc.at_least(j, SHIFT, 2):
                            act.wait_ge(s_floors, e - 1)
                        src = x2[:, ds(slot(oc, j), 1), :, SUB * s:SUB * (s + 1)].rearrange("p a c t -> p t (a c)")
                        A.activation(halves2[s % 2][:, :].rearrange("p (t c) -> p t c", c=C), src, ACT.Copy,
                                     scale=2.0, bias=-0.5).then_inc(s_halves2, 1)

            act.wait_ge(setup_dve, SETUP)
            octets(act, images, body)

        @block.vector
        def _(dve):
            V = nc.vector
            done = [0]

            def link(ins):
                done[0] += 1
                ins.then_inc(setup_dve, 1)
                dve.wait_ge(setup_dve, done[0])

            both = params[:, :].rearrange("p (n k) -> p k n", n=2)
            dve.wait_ge(consts_in, 16 * 6)
            link(V.tensor_scalar(norm[:, 0:2], both[:, 4, :], BN_EPS, None, ALU.add))
            link(V.memset(norm[:, 6:8], -0.5))
            dve.wait_ge(setup_pool, 1)
            link(V.tensor_tensor(norm[:, 4:6], both[:, 1, :], norm[:, 2:4], ALU.mult))
            link(V.tensor_tensor(norm[:, 2:4], both[:, 3, :], norm[:, 4:6], ALU.mult))
            link(V.tensor_tensor(norm[:, 6:8], both[:, 0, :], norm[:, 4:6], ALU.mult))
            link(V.tensor_tensor(norm[:, 2:4], both[:, 2, :], norm[:, 2:4], ALU.subtract))
            link(V.tensor_tensor(norm[:, 0:2], norm[:, 6:8], norm[:, 2:4], ALU.add))
            link(V.tensor_copy(ident_bf[:, :], ident[:, :]))
            link(V.tensor_copy(ident_hf[:, :], ident[:, :]))
            for i in range(3):
                link(V.tensor_copy(w_part[i][:, :], w_rest[:, :]))
                if i < 2:
                    link(V.tensor_tensor(w_rest[:, :], w_rest[:, :], w_part[i][:, :], ALU.subtract))
            link(V.memset(kmax[:, :], 0.0))
            link(V.memset(dom[:, :], 0.0))
            link(V.memset(pat[:, :], 0.0))
            assert done[0] == SETUP, done[0]

            def words(t, n):
                return t[:, :].rearrange("p (t w c) -> p w t c", w=n, c=GC)

            def shifted(dst, src, by, mask):
                op = ALU.logical_shift_left if by >= 0 else ALU.logical_shift_right
                return V.tensor_scalar(dst, src.rearrange("p (t c) -> p t c", c=GC), abs(by), mask, op, ALU.bitwise_and)

            def body(oc):
                o = oc.o
                for j in range(STEPS):
                    stage1 = oc.exists(j, 0, n1)
                    if stage1:
                        i, b = oc.count(j, 0), j % 2
                        base = i * 6
                        dve.wait_ge(s_prep, i + 1)
                        V.tensor_scalar(clipped[:, :], halves[b][:, :], 511.0, 32.0, ALU.min, ALU.add)\
                            .then_inc(s_codes, 1)
                        dve.wait_ge(s_codes, base + 1)
                        V.tensor_tensor(code[:, :], clipped[:, :], inrange[b][:, :], ALU.mult).then_inc(s_codes, 1)
                    if oc.exists(j, SHIFT + 1, n1):
                        e = oc.count(j, SHIFT + 1)
                        dve.wait_ge(s_turned, e + 1)
                        if oc.at_least(j, SHIFT + 1, 1):
                            dve.wait_ge(s_conv1, e * 2)
                        if j == 5:
                            dve.wait_ge(s_pat, oc.image if oc.rep < images * OCTETS else images)
                        V.tensor_scalar(att[:, :], turned[:, :], pat[:, 0:1], None, ALU.not_equal).then_inc(s_att, 1)
                    if stage1:
                        if oc.at_least(j, 0, 1):
                            dve.wait_ge(s_onehots, i)
                        dve.wait_ge(s_codes, base + 2)
                        V.tensor_scalar(high[:, :], code[:, :], 2, 0xF80, ALU.logical_shift_left, ALU.bitwise_and)\
                            .then_inc(s_codes, 1)
                        V.tensor_scalar(low[:, :], code[:, :], 6, 0x780, ALU.logical_shift_left, ALU.bitwise_and)\
                            .then_inc(s_codes, 1)
                        dve.wait_ge(s_codes, base + 3)
                        V.tensor_scalar(high[:, :], high[:, :].bitcast(bf16), 2.0 ** 126, None, ALU.mult)\
                            .then_inc(s_codes, 1)
                        dve.wait_ge(s_codes, base + 4)
                        V.tensor_scalar(low[:, :], low[:, :].bitcast(bf16), 2.0 ** 127, 1.0, ALU.mult, ALU.max)\
                            .then_inc(s_codes, 1)
                    if j == KEY_STEP and oc.exists(0, STEPS, n1):
                        dve.wait_ge(s_totals, o * STEPS)
                        if oc.rep > 1:
                            dve.wait_ge(s_best, o - 1)
                        for a, unit in ((0, 256.0 * 1024.0), (1, 256.0)):
                            V.scalar_tensor_tensor(out=key[:, :, WN * a:WN * (a + 1)], in0=totals[:, a, :, :],
                                                   scalar=unit, in1=keys[:, :, WN * a:WN * (a + 1)],
                                                   op0=ALU.mult, op1=ALU.add).then_inc(s_key, 1)
                        dve.wait_ge(s_key, o * 2)
                        if oc.rep > OCTETS and oc.rep % OCTETS == 1:
                            dve.wait_ge(s_bestT, oc.image)
                        V.tensor_reduce(best[:, ds(((o + 3) % OCTETS) * 2, 2)], key[:, :, :], axis=AX.X,
                                        op=ALU.max).then_inc(s_best, 1)
                    dec = oc.rep % OCTETS == 0 and OCTETS <= oc.rep <= images * OCTETS
                    if dec and j == TURN_STEP + 1:
                        m4 = oc.image * 4 - 4
                        dve.wait_ge(s_bestT, oc.image)
                        V.tensor_reduce(kmax[:, :], decode[0:GC, 0:P].rearrange("g (w c b) -> g c w b", c=GC, b=2),
                                        axis=AX.XY, op=ALU.max).then_inc(s_dec, 1)
                        dve.wait_ge(s_dec, m4 + 1)
                        V.tensor_copy(kint[:, :], kmax[:, :]).then_inc(s_dec, 1)
                        dve.wait_ge(s_dec, m4 + 2)
                        V.tensor_scalar(kbin[:, :], kint[:, :], 255, 255, ALU.bitwise_and, ALU.bitwise_xor)\
                            .then_inc(s_dec, 1)
                        dve.wait_ge(s_dec, m4 + 3)
                        V.tensor_copy(kval[:, :], kbin[:, :]).then_inc(s_dec, 1)
                    if dec and j == TURN_STEP + 2:
                        m3 = oc.image * 3 - 3
                        dve.wait_ge(s_spread, oc.image)
                        V.tensor_tensor(spread[:, :], decode[:, P:P + GC], pick[:, P:P + GC], ALU.mult)\
                            .then_inc(s_pat2, 1)
                        dve.wait_ge(s_pat2, m3 + 1)
                        V.tensor_reduce(dom[:, :], spread[:, :], axis=AX.X, op=ALU.add).then_inc(s_pat2, 1)
                        dve.wait_ge(s_pat2, m3 + 2)
                        V.tensor_scalar(pat_lo[:, :], dom[:, :], 1.0 / 64, 2.0, ALU.mult, ALU.add).then_inc(s_pat2, 1)
                        dve.wait_ge(s_pat2, m3 + 3)
                        V.scalar_tensor_tensor(out=pat[:, :], in0=dom[:, :], scalar=1.0 / 32, in1=pat_lo[:, :],
                                               op0=ALU.mult, op1=ALU.max).then_inc(s_pat, 1)
                    if stage1:
                        if oc.at_least(j, 0, 2):
                            dve.wait_ge(s_hist, i - 1)
                        dve.wait_ge(s_codes, base + 5)
                        for h in range(NH):
                            shifted(words(onehot_h[b], NH)[:, h], high[:, :], 6 - h, 0x4040)
                    if oc.exists(j, SHIFT, n1):
                        e, s = oc.count(j, SHIFT), (j - SHIFT) % STEPS
                        dve.wait_ge(s_halves2, e + 1)
                        if oc.at_least(j, SHIFT, 2):
                            dve.wait_ge(s_turned, e - 1)
                        V.tensor_scalar(floors[s % 2][:, :], halves2[s % 2][:, :], 0.5, 16384 - 0.25,
                                        ALU.mult, ALU.add).then_inc(s_floors, 1)
                    if stage1:
                        dve.wait_ge(s_codes, base + 6)
                        for n, l in enumerate(LOWS):
                            last = shifted(words(onehot_l[b], NL)[:, n], low[:, :], 4 - l, 0x5050)
                        last.then_inc(s_onehots, 1)
                    if oc.exists(j, 1, n1):
                        i = oc.count(j, 1)
                        dve.wait_ge(s_bigint, i + 1)
                        if oc.at_least(j, 1, 1):
                            dve.wait_ge(s_totals, i)
                        V.scalar_tensor_tensor(out=small[:, :], in0=big_int[:, :], scalar=-4.0,
                                               in1=counts[(j - 1) % 2][:, :], op0=ALU.mult, op1=ALU.add)\
                            .then_inc(s_small, 1)
                    if j < 4 and oc.exists(0, (OCTETS + 2) * STEPS, n1):
                        c = o - (OCTETS + 2)
                        if j == 0:
                            dve.wait_ge(s_gate, c + 1)
                        if oc.rep > OCTETS + 2 or j >= 2:
                            dve.wait_ge(stored[j % 2], (c * 2 + j // 2) * 16)
                        ch = C // 4
                        V.tensor_tensor(product[j % 2][:, :, :],
                                        x2[:, ds(o % 2, 1), ch * j:ch * (j + 1), :].rearrange("p a c t -> p (a c) t"),
                                        gate[:, :].rearrange("p (a t) -> p a t", a=1).broadcast_to([P, ch, COLS]),
                                        ALU.mult).then_inc(s_product, 1)

            octets(dve, images, body)

        @block.tensor
        def _(pe):
            T = nc.tensor

            def body(oc):
                o = oc.o
                for j in range(STEPS):
                    dec = oc.rep % OCTETS == 0 and OCTETS <= oc.rep <= images * OCTETS
                    if dec and j == TURN_STEP:
                        pe.wait_ge(s_best, o)
                        T.transpose(decode[0:GC, 0:P], best[:, :], ident[:, :]).then_inc(s_bestT, 1)
                    if dec and j == TURN_STEP + 1:
                        pe.wait_ge(s_dec, oc.image * 4)
                        T.matmul(decode[:, P:P + GC], pick[0:GC, 0:P], kval[:, :], start=True, stop=True)\
                            .then_inc(s_spread, 1)
                    if oc.exists(j, SHIFT, n1):
                        e, s = oc.count(j, SHIFT), (j - SHIFT) % STEPS
                        pe.wait_ge(s_floors, e + 1)
                        if oc.at_least(j, SHIFT, 1):
                            pe.wait_ge(s_att, e)
                        q = floors[s % 2][:, :].bitcast(bf16)
                        for k in range(SUB // 2):
                            last = T.transpose(turned[:, P * k:P * (k + 1)], q[:, P * k:P * (k + 1)], ident_bf[:, :])
                        last.then_inc(s_turned, 1)
                    if oc.exists(j, SHIFT + 1, n1):
                        e = oc.count(j, SHIFT + 1)
                        pe.wait_ge(s_att, e + 1)
                        for h in range(2):
                            if oc.at_least(j, SHIFT + 1, 1):
                                pe.wait_ge(s_hidden, e * 2 + (h - 1))
                            for n in range(3):
                                last = T.matmul(pre[h][:, :], w_part[n][:, :], att[:, 512 * h:512 * (h + 1)],
                                                start=n == 0, stop=n == 2)
                            last.then_inc(s_conv1, 1)
                    if oc.exists(j, 0, n1):
                        i, b = oc.count(j, 0), j % 2
                        pe.wait_ge(s_onehots, i + 1)
                        if oc.at_least(j, 0, 2):
                            pe.wait_ge(s_small, i - 1)
                        pe.sem_inc(hist_begun, 1)
                        oh, ol = onehot_h[b][:, :].bitcast(fp8), onehot_l[b][:, :].bitcast(fp8)
                        for t in range(COLS):
                            k = t // PACK
                            last = T.matmul(counts[b][:, WN * k:WN * (k + 1)], oh[:, WM * t:WM * (t + 1)],
                                            ol[:, WN * t:WN * (t + 1)], start=t % PACK == 0, stop=t % PACK == PACK - 1)
                        last.then_inc(s_hist, 1)
                    if oc.exists(j, 1, n1):
                        i, s = oc.count(j, 1), (j - 1) % STEPS
                        pe.wait_ge(s_small, i + 1)
                        pe.wait_ge(s_big, i + 1)
                        if s == 0 and oc.at_least(j, 1, STEPS):
                            pe.wait_ge(s_key, o * 2)
                        for a, part in ((0, small), (1, big)):
                            for k in range(PARTS):
                                last = T.matmul(totals[:, a, s // 4, :], ident_hf[:, :], part[:, WN * k:WN * (k + 1)],
                                                start=s == 0 and a == 0 and k == 0,
                                                stop=s % 4 == 3 and k == PARTS - 1, skip_group_check=True)
                        last.then_inc(s_totals, 1)
                    if oc.exists(j, SHIFT + 1, n1):
                        e, s = oc.count(j, SHIFT + 1), (j - SHIFT - 1) % STEPS
                        pe.wait_ge(s_hidden, e * 2 + 2)
                        if s == 0 and oc.at_least(j, SHIFT + 1, STEPS):
                            pe.wait_ge(s_gate, o - OCTETS)
                        for k in range(SUB // 2):
                            col = SUB * s + 2 * k
                            last = T.matmul(logit[:, col:col + 2], hidden[:, P * k:P * (k + 1)], w2[:, :],
                                            start=True, stop=True)
                        last.then_inc(s_conv2, 1)

            pe.wait_ge(setup_dve, SETUP)
            octets(pe, images, body)


def constants():
    import numpy as np
    ident = np.eye(P, dtype=np.float32)
    m = np.arange(P)
    hi = m // 16 + 8 * (m % 2)
    ch = (m % 16) // 2
    n = np.arange(2 * NL * GC)
    keys = np.zeros((P, 2, 2, 2 * NL * GC), np.float32)
    for a in range(2):
        lo = np.array(LOWS)[n // 16] + 8 * (n % 2) + 2 * a
        same = ch[:, None] == ((n % 16) // 2)[None, :]
        k = (255 - (16 * hi[:, None] + lo[None, :])) - (1 << 23)
        keys[:, :, a, :] = np.where(same, k, -(1 << 25))[:, None, :]
    pick = np.zeros((P, P + GC), np.float32)
    for p in range(P):
        pick[(p % C) // GC, p] = 1
        pick[p, P + p % GC] = 1
    return ident, keys.reshape(P, -1), pick


def kernel(**inputs):
    import numpy as np
    import concourse.bacc as bacc
    from concourse.bass_utils import run_bass_kernel_spmd

    x = np.asarray(inputs["x"])
    images = x.shape[0]
    vec = {k.removeprefix("L0_conv_"): np.asarray(v) for k, v in inputs.items() if k != "x"}
    w1t = np.zeros((P, P), np.float32)
    w2b = np.zeros((P, 2), np.float32)
    for h in range(2):
        w1t[C * h:C * (h + 1), C * h:C * (h + 1)] = vec["conv1_w"].T
        w2b[C * h:C * (h + 1), h] = vec["conv2_w"][0]
    par = np.zeros((P, 10), np.float32)
    for k, name in enumerate(("conv1_b", "bn1_gamma", "bn1_beta", "bn1_mean", "bn1_var")):
        par[0:C, k] = vec[name]
        par[C:P, k] = vec[name]
    for k, name in enumerate(("conv2_b", "bn2_gamma", "bn2_beta", "bn2_mean", "bn2_var")):
        par[:, 5 + k] = vec[name][0]
    ident, keys, pick = constants()
    arrays = {"in_x": np.ascontiguousarray(x).reshape(images * C, PIX), "in_w1t": w1t, "in_w2": w2b, "in_par": par,
              "in_ident": ident, "in_keys": keys, "in_pick": pick}
    nc = bacc.Bacc("TRN2", target_bir_lowering=False, num_devices=1)
    aps = [nc.dram_tensor(k, a.shape, mybir.dt.float32, kind="ExternalInput").ap() for k, a in arrays.items()]
    out = nc.dram_tensor("out_y", (images * C, PIX), mybir.dt.float32, kind="ExternalOutput").ap()
    build(nc, *aps, out, float(np.float32(256 / 255.0)))
    r = run_bass_kernel_spmd(nc, [arrays], core_ids=[0])
    return r.results[0]["out_y"].reshape(x.shape)
```

```python
import concourse.bass as bass
from concourse import mybir
from contextlib import ExitStack

C = 64
PIX = 256 * 256
P = 128
GC = 8
COLS = 128
ROW = PIX // P
QUARTERS = ROW // COLS
STEPS = 8
OCTETS = 4
SUB = COLS // STEPS
SHIFT = OCTETS * STEPS + 4
PACK = 16
PARTS = COLS // PACK
NH = 8
LOWS = (0, 1, 4, 5)
NL = len(LOWS)
BN_EPS = 1e-5



class Octet:

    def __init__(self, o, rep, image=0):
        self.o, self.rep, self.image = o, rep, image

    def count(self, step, lag):
        return self.o * STEPS + (step - lag)

    def exists(self, step, lag, total):
        return 0 <= self.rep * STEPS + step - lag < total

    def at_least(self, step, lag, least):
        return self.rep * STEPS + step - lag >= least


def octets(eng, images, body):
    total = images * OCTETS
    body(Octet(0, 0))
    with eng.Fori(1, OCTETS) as q:
        body(Octet(q, 1))
    body(Octet(OCTETS, OCTETS, 1))
    body(Octet(OCTETS + 1, OCTETS + 1, 1))
    with eng.Fori(OCTETS + 2, 2 * OCTETS) as q:
        body(Octet(q, OCTETS + 2, 1))
    with eng.Fori(2, images) as n:
        body(Octet(n * OCTETS, 2 * OCTETS, n))
        with eng.Fori(1, OCTETS) as q:
            body(Octet(n * OCTETS + q, 2 * OCTETS + 1, n))
    body(Octet(total, total, images))
    with eng.Fori(total + 1, total + OCTETS) as q:
        body(Octet(q, total + 1))
    body(Octet(total + OCTETS, total + OCTETS))
    body(Octet(total + OCTETS + 1, total + OCTETS + 1))


def build(nc, x, w1t, w2b, par, ident_in, keys_in, pick_in, out, bin_scale):
    fp32, bf16, fp16 = mybir.dt.float32, mybir.dt.bfloat16, mybir.dt.float16
    fp8, u16, i16, i32 = mybir.dt.float8e5, mybir.dt.uint16, mybir.dt.int16, mybir.dt.int32
    ALU, ACT, AX = mybir.AluOpType, mybir.ActivationFunctionType, mybir.AxisListType
    ds = bass.ds

    images = x.shape[0] // C
    n1 = images * OCTETS * STEPS
    N = GC * COLS
    ctx = ExitStack()
    with ctx:
        def sb(name, shape, dt):
            return ctx.enter_context(nc.sbuf_tensor(name, shape, dt))

        def pb(name, shape, dt):
            return ctx.enter_context(nc.psum_tensor(name, shape, dt))

        def sem(name):
            return ctx.enter_context(nc.semaphore(name))

        x1 = [sb(f"x1_{g}", [P, GC, ROW], fp32) for g in range(2)]
        scaled = sb("scaled", [P, N], fp32)
        quanta = [sb(f"quanta{i}", [P, N], i16) for i in range(2)]
        above = [sb(f"above{i}", [P, N], i16) for i in range(2)]
        code = sb("code", [P, N], i16)
        high_bits = sb("high_bits", [P, N], u16)
        high = [sb(f"high{i}", [P, N], u16) for i in range(2)]
        low = sb("low", [P, N], u16)
        onehot_h = [sb(f"onehot_h{i}", [P, N * NH], u16) for i in range(2)]
        onehot_l = [sb(f"onehot_l{i}", [P, N * NL], u16) for i in range(2)]
        WM, WN = 2 * NH * GC, 2 * NL * GC
        big_int = sb("big_int", [P, PARTS * WN], i16)
        big = sb("big", [P, PARTS * WN], fp16)
        small = sb("small", [P, PARTS * WN], fp16)
        key = sb("key", [P, 2, 2 * WN], fp32)
        best = sb("best", [P, 2 * OCTETS], fp32)
        kmax = sb("kmax", [GC, GC], fp32)
        kint = sb("kint", [GC, GC], i32)
        kbin = sb("kbin", [GC, GC], i32)
        kval = sb("kval", [GC, GC], fp32)
        spread = sb("spread", [P, GC], fp32)
        dom = sb("dom", [P, 1], fp32)
        pat_lo = sb("pat_lo", [P, 1], fp32)
        pat = sb("pat", [P, 1], fp32)
        x2 = sb("x2", [P, 2, C, COLS], fp32)
        halves2 = [sb(f"halves2_{i}", [P, C * SUB], i16) for i in range(2)]
        floors = [sb(f"floors{i}", [P, C * SUB], i16) for i in range(2)]
        att = sb("att", [P, C * SUB], bf16)
        hidden = sb("hidden", [P, C * SUB], fp32)
        gate = sb("gate", [P, COLS], fp32)
        product = [sb(f"product{i}", [P, C // 4, COLS], fp32) for i in range(2)]
        ident = sb("ident", [P, P], fp32)
        ident_bf = sb("ident_bf", [P, P], bf16)
        ident_hf = sb("ident_hf", [P, P], fp16)
        keys = sb("keys", [P, 2, 2 * WN], fp32)
        pick = sb("pick", [P, P + GC], fp32)
        w_rest = sb("w_rest", [P, P], fp32)
        w_part = [sb(f"w_part{i}", [P, P], bf16) for i in range(3)]
        w2 = sb("w2", [P, 2], fp32)
        params = sb("params", [P, 10], fp32)
        minus_half = sb("minus_half", [P, 1], fp32)
        norm = sb("norm", [P, 8], fp32)

        counts = [pb(f"counts{i}", [P, PARTS * WN], fp32) for i in range(2)]
        totals = pb("totals", [P, 2, 2, WN], fp32)
        turned = pb("turned", [P, C * SUB], bf16)
        pre = pb("pre", [P, C * SUB], fp32)
        logit = pb("logit", [P, 512], fp32)
        decode = pb("decode", [P, 512], fp32)

        consts_in = sem("consts_in")
        x1_in = [sem(f"x1_in{g}") for g in range(2)]
        x2_in = [sem(f"x2_in{k}") for k in range(4)]
        stored = [sem(f"stored{i}") for i in range(2)]
        setup_dve = sem("setup_dve")
        setup_pool = sem("setup_pool")
        s_scaled, s_prep, s_code = sem("scaled_done"), sem("prep_done"), sem("code_ready")
        s_highbits, s_high, s_lowbits, s_low = sem("high_bits_ready"), sem("high_ready"), sem("low_bits_ready"), sem("low_ready")
        s_onehots, s_hist = sem("onehots_ready"), sem("hist_done")
        s_bigint, s_big, s_small = sem("bigint_ready"), sem("big_ready"), sem("small_ready")
        s_totals, s_key, s_best = sem("totals_done"), sem("key_ready"), sem("best_ready")
        s_bestT, s_dec, s_spread, s_pat = sem("best_turned"), sem("bins_chain"), sem("bins_spread"), sem("pat_ready")
        hist_begun = sem("hist_begun")
        s_pat2 = sem("pat_chain")
        s_halves2, s_floors, s_turned = sem("halves2_ready"), sem("floors_ready"), sem("turned_done")
        s_att, s_conv1, s_hidden = sem("att_ready"), sem("conv1_done"), sem("hidden_ready")
        s_conv2, s_gate, s_product = sem("conv2_done"), sem("gate_ready"), sem("product_ready")

        block = ctx.enter_context(nc.Block())
        SETUP = 17
        KEY_STEP, TURN_STEP = 3, 3

        def slot(oc, step):
            return oc.o % 2 if step >= 4 else (oc.o + 1) % 2

        @block.sync
        def _(sp):
            for dst, src in ((ident, ident_in), (pick, pick_in), (w_rest, w1t), (w2, w2b), (params, par)):
                sp.dma_start(dst[:, :], src).then_inc(consts_in, 16)
            sp.dma_start(keys[:, :, :], keys_in.rearrange("p (a b) -> p a b", a=2)).then_inc(consts_in, 16)

            def chunk(t, c, k):
                rows = t[ds((c // QUARTERS) * C + C // 4 * k, C // 4), :].rearrange("c (p t) -> p c t", p=P)
                return rows[:, :, ds((c % QUARTERS) * COLS, COLS)]

            def body(oc):
                o = oc.o
                ch = C // 4
                for g in range(2):
                    if oc.exists(0, 0, n1):
                        if oc.rep > 0:
                            sp.wait_ge(s_prep, o * STEPS - STEPS + 4 * (g + 1))
                        src = x[ds((o * 2 + g) * GC, GC), :].rearrange("c (p t) -> p c t", p=P)
                        sp.dma_start(x1[g][:, :, :], src).then_inc(x1_in[g], 16)
                    for k in (2 * g, 2 * g + 1):
                        if oc.rep >= OCTETS + 2:
                            c = o - (OCTETS + 2)
                            sp.wait_ge(s_product, c * 4 + (k + 1))
                            sp.dma_start(chunk(out, c, k), product[k % 2][:, :, :]).then_inc(stored[k % 2], 16)
                        if oc.rep >= OCTETS and oc.rep < (images + 1) * OCTETS:
                            c = o - OCTETS
                            sp.dma_start(x2[:, ds(o % 2, 1), ch * k:ch * (k + 1), :].rearrange("p a c t -> p (a c) t"),
                                         chunk(x, c, k)).then_inc(x2_in[k], 16)

            octets(sp, images, body)
            for i in range(2):
                sp.wait_ge(stored[i], 16 * 2 * images * QUARTERS)

        @block.gpsimd
        def _(pool):
            pool.wait_ge(setup_dve, 2)
            nc.gpsimd.tensor_tensor(norm[:, 2:4], norm[:, 0:2], norm[:, 6:8], ALU.pow).then_inc(setup_pool, 1)

        @block.scalar
        def _(act):
            A = nc.scalar

            def by_column(t):
                return t.rearrange("p c t -> p t c")

            def body(oc):
                o = oc.o
                for j in range(STEPS):
                    if oc.exists(j, 0, n1):
                        i, b = oc.count(j, 0), j % 2
                        if j % 4 == 0:
                            act.wait_ge(x1_in[j // 4], (o + 1) * 16)
                        if oc.at_least(j, 0, 2):
                            act.wait_ge(s_code, i - 1)
                        src = by_column(x1[j // 4][:, :, COLS * (j % 4):COLS * (j % 4 + 1)])
                        A.activation(above[b][:, :].rearrange("p (t c) -> p t c", c=GC), src, ACT.Sign,
                                     bias=-(255.0 + 2.0 ** -16))
                        if oc.at_least(j, 0, 1):
                            act.wait_ge(s_prep, i)
                        A.activation(scaled[:, :].rearrange("p (t c) -> p t c", c=GC), src, ACT.Copy,
                                     scale=128.0 * bin_scale).then_inc(s_scaled, 1)
                        act.wait_ge(s_scaled, i + 1)
                        A.activation(quanta[b][:, :], scaled[:, :], ACT.Copy, bias=-0.5).then_inc(s_prep, 1)
                    if j == 7 and oc.exists(0, (OCTETS + 1) * STEPS, n1):
                        c = o - (OCTETS + 1)
                        act.wait_ge(s_conv2, (c + 1) * STEPS)
                        if oc.rep > OCTETS + 1:
                            act.wait_ge(s_product, c * 4)
                        A.activation(gate[:, :], logit[:, 0:COLS], ACT.Sigmoid,
                                     scale=norm[:, 5:6], bias=norm[:, 1:2]).then_inc(s_gate, 1)
                    if oc.exists(j, 1, n1):
                        i = oc.count(j, 1)
                        act.wait_ge(s_highbits, i + 1)
                        if oc.at_least(j, 1, 2):
                            act.wait_ge(s_onehots, i - 1)
                        A.activation(high[(j - 1) % 2][:, :], high_bits[:, :].bitcast(bf16), ACT.Copy,
                                     scale=2.0 ** 111).then_inc(s_high, 1)
                    if oc.exists(j, SHIFT + 3, n1):
                        e = oc.count(j, SHIFT + 3)
                        act.wait_ge(s_conv1, e + 1)
                        if oc.at_least(j, SHIFT + 3, 1):
                            act.wait_ge(s_conv2, e)
                        A.activation(hidden[:, :], pre[:, :], ACT.Relu,
                                     scale=norm[:, 4:5], bias=norm[:, 0:1]).then_inc(s_hidden, 1)
                    if oc.exists(j, 3, n1):
                        i = oc.count(j, 3)
                        act.wait_ge(s_hist, i + 1)
                        if oc.at_least(j, 3, 1):
                            act.wait_ge(s_small, i)
                            act.wait_ge(s_totals, i)
                        A.activation(big_int[:, :], counts[(j - 3) % 2][:, :], ACT.Copy, scale=0.25).then_inc(s_bigint, 1)
                        act.wait_ge(s_bigint, i + 1)
                        A.activation(big[:, :], big_int[:, :], ACT.Copy).then_inc(s_big, 1)
                    if oc.exists(j, SHIFT, n1):
                        e, s = oc.count(j, SHIFT), (j - SHIFT) % STEPS
                        if s == 0:
                            for k in range(4):
                                act.wait_ge(x2_in[k], (o - OCTETS + 1) * 16)
                        if oc.at_least(j, SHIFT, 2):
                            act.wait_ge(s_floors, e - 1)
                        src = x2[:, ds(slot(oc, j), 1), :, SUB * s:SUB * (s + 1)].rearrange("p a c t -> p t (a c)")
                        A.activation(halves2[s % 2][:, :].rearrange("p (t c) -> p t c", c=C), src, ACT.Copy,
                                     scale=2.0, bias=-0.5).then_inc(s_halves2, 1)

            act.wait_ge(setup_dve, SETUP)
            octets(act, images, body)

        @block.vector
        def _(dve):
            V = nc.vector
            done = [0]

            def link(ins):
                done[0] += 1
                ins.then_inc(setup_dve, 1)
                dve.wait_ge(setup_dve, done[0])

            both = params[:, :].rearrange("p (n k) -> p k n", n=2)
            dve.wait_ge(consts_in, 16 * 6)
            link(V.tensor_scalar(norm[:, 0:2], both[:, 4, :], BN_EPS, None, ALU.add))
            link(V.memset(norm[:, 6:8], -0.5))
            dve.wait_ge(setup_pool, 1)
            link(V.tensor_tensor(norm[:, 4:6], both[:, 1, :], norm[:, 2:4], ALU.mult))
            link(V.tensor_tensor(norm[:, 2:4], both[:, 3, :], norm[:, 4:6], ALU.mult))
            link(V.tensor_tensor(norm[:, 6:8], both[:, 0, :], norm[:, 4:6], ALU.mult))
            link(V.tensor_tensor(norm[:, 2:4], both[:, 2, :], norm[:, 2:4], ALU.subtract))
            link(V.tensor_tensor(norm[:, 0:2], norm[:, 6:8], norm[:, 2:4], ALU.add))
            link(V.tensor_copy(ident_bf[:, :], ident[:, :]))
            link(V.tensor_copy(ident_hf[:, :], ident[:, :]))
            for i in range(3):
                link(V.tensor_copy(w_part[i][:, :], w_rest[:, :]))
                if i < 2:
                    link(V.tensor_tensor(w_rest[:, :], w_rest[:, :], w_part[i][:, :], ALU.subtract))
            link(V.memset(kmax[:, :], 0.0))
            link(V.memset(dom[:, :], 0.0))
            link(V.memset(pat[:, :], 0.0))
            assert done[0] == SETUP, done[0]

            def words(t, n):
                return t[:, :].rearrange("p (t w c) -> p w t c", w=n, c=GC)

            def shifted(dst, src, by, mask):
                op = ALU.logical_shift_left if by >= 0 else ALU.logical_shift_right
                return V.tensor_scalar(dst, src.rearrange("p (t c) -> p t c", c=GC), abs(by), mask, op, ALU.bitwise_and)

            def body(oc):
                o = oc.o
                for j in range(STEPS):
                    dec = oc.rep % OCTETS == 0 and OCTETS <= oc.rep <= images * OCTETS
                    if oc.exists(j, 0, n1):
                        i, b = oc.count(j, 0), j % 2
                        dve.wait_ge(s_prep, i + 1)
                        if oc.at_least(j, 0, 1):
                            dve.wait_ge(s_lowbits, i)
                        V.tensor_tensor(code[:, :], quanta[b][:, :], above[b][:, :], ALU.bitwise_xor)\
                            .then_inc(s_code, 1)
                    if dec and j == TURN_STEP + 2:
                        m3 = oc.image * 3 - 3
                        dve.wait_ge(s_spread, oc.image)
                        V.tensor_tensor(spread[:, :], decode[:, P:P + GC], pick[:, P:P + GC], ALU.mult)\
                            .then_inc(s_pat2, 1)
                        dve.wait_ge(s_pat2, m3 + 1)
                        V.tensor_reduce(dom[:, :], spread[:, :], axis=AX.X, op=ALU.add).then_inc(s_pat2, 1)
                        dve.wait_ge(s_pat2, m3 + 2)
                        V.tensor_scalar(pat_lo[:, :], dom[:, :], 1.0 / 64, 2.0, ALU.mult, ALU.add).then_inc(s_pat2, 1)
                        dve.wait_ge(s_pat2, m3 + 3)
                        V.scalar_tensor_tensor(out=pat[:, :], in0=dom[:, :], scalar=1.0 / 32, in1=pat_lo[:, :],
                                               op0=ALU.mult, op1=ALU.max).then_inc(s_pat, 1)
                    if oc.exists(j, SHIFT + 1, n1):
                        e = oc.count(j, SHIFT + 1)
                        dve.wait_ge(s_turned, e + 1)
                        if oc.at_least(j, SHIFT + 1, 1):
                            dve.wait_ge(s_conv1, e)
                        if j == 5:
                            dve.wait_ge(s_pat, oc.image if oc.rep < images * OCTETS else images)
                        V.tensor_scalar(att[:, :], turned[:, :], pat[:, 0:1], None, ALU.not_equal).then_inc(s_att, 1)
                    if oc.exists(j, 0, n1):
                        dve.wait_ge(s_code, i + 1)
                        if oc.at_least(j, 0, 1):
                            dve.wait_ge(s_high, i)
                        V.tensor_scalar(high_bits[:, :], code[:, :].bitcast(u16), 4, 0xF80,
                                        ALU.logical_shift_right, ALU.bitwise_and).then_inc(s_highbits, 1)
                    if j == KEY_STEP and oc.exists(0, STEPS, n1):
                        dve.wait_ge(s_totals, o * STEPS)
                        if oc.rep > 1:
                            dve.wait_ge(s_best, o - 1)
                        for a, unit in ((0, 256.0 * 1024.0), (1, 256.0)):
                            V.scalar_tensor_tensor(out=key[:, :, WN * a:WN * (a + 1)], in0=totals[:, a, :, :],
                                                   scalar=unit, in1=keys[:, :, WN * a:WN * (a + 1)],
                                                   op0=ALU.mult, op1=ALU.add).then_inc(s_key, 1)
                        dve.wait_ge(s_key, o * 2)
                        if oc.rep > OCTETS and oc.rep % OCTETS == 1:
                            dve.wait_ge(s_bestT, oc.image)
                        V.tensor_reduce(best[:, ds(((o + 3) % OCTETS) * 2, 2)], key[:, :, :], axis=AX.X,
                                        op=ALU.max).then_inc(s_best, 1)
                    if dec and j == TURN_STEP + 1:
                        m4 = oc.image * 4 - 4
                        dve.wait_ge(s_bestT, oc.image)
                        V.tensor_reduce(kmax[:, :], decode[0:GC, 0:P].rearrange("g (w c b) -> g c w b", c=GC, b=2),
                                        axis=AX.XY, op=ALU.max).then_inc(s_dec, 1)
                        dve.wait_ge(s_dec, m4 + 1)
                        V.tensor_copy(kint[:, :], kmax[:, :]).then_inc(s_dec, 1)
                        dve.wait_ge(s_dec, m4 + 2)
                        V.tensor_scalar(kbin[:, :], kint[:, :], 255, 255, ALU.bitwise_and, ALU.bitwise_xor)\
                            .then_inc(s_dec, 1)
                        dve.wait_ge(s_dec, m4 + 3)
                        V.tensor_copy(kval[:, :], kbin[:, :]).then_inc(s_dec, 1)
                    if oc.exists(j, 1, n1):
                        i1, b1 = oc.count(j, 1), (j - 1) % 2
                        dve.wait_ge(s_high, i1 + 1)
                        if oc.at_least(j, 1, 2):
                            dve.wait_ge(s_hist, i1 - 1)
                        for h in range(NH):
                            shifted(words(onehot_h[b1], NH)[:, h], high[b1][:, :], 6 - h, 0x4040)
                    if oc.exists(j, SHIFT, n1):
                        e, s = oc.count(j, SHIFT), (j - SHIFT) % STEPS
                        dve.wait_ge(s_halves2, e + 1)
                        if oc.at_least(j, SHIFT, 2):
                            dve.wait_ge(s_turned, e - 1)
                        V.tensor_scalar(floors[s % 2][:, :], halves2[s % 2][:, :], 0.5, 16384 - 0.25,
                                        ALU.mult, ALU.add).then_inc(s_floors, 1)
                    if oc.exists(j, 1, n1):
                        dve.wait_ge(s_low, i1 + 1)
                        for n, l in enumerate(LOWS):
                            last = shifted(words(onehot_l[b1], NL)[:, n], low[:, :], 4 - l, 0x5050)
                        last.then_inc(s_onehots, 1)
                    if oc.exists(j, 0, n1):
                        if oc.at_least(j, 0, 1):
                            dve.wait_ge(s_onehots, i)
                        V.tensor_scalar(low[:, :], code[:, :].bitcast(u16), 0x780, None, ALU.bitwise_and)\
                            .then_inc(s_lowbits, 1)
                    if oc.exists(j, 2, n1):
                        i = oc.count(j, 2)
                        dve.wait_ge(s_bigint, i + 1)
                        if oc.at_least(j, 2, 1):
                            dve.wait_ge(s_totals, i)
                        V.scalar_tensor_tensor(out=small[:, :], in0=big_int[:, :], scalar=-4.0,
                                               in1=counts[(j - 2) % 2][:, :], op0=ALU.mult, op1=ALU.add)\
                            .then_inc(s_small, 1)
                    if oc.exists(j, 0, n1):
                        dve.wait_ge(s_lowbits, oc.count(j, 0) + 1)
                        V.tensor_scalar(low[:, :], low[:, :].bitcast(bf16), 2.0 ** 127, 1.0, ALU.mult, ALU.max)\
                            .then_inc(s_low, 1)
                    k = (j - 6) % STEPS
                    if k < 4 and oc.exists(j, (OCTETS + 1) * STEPS + 6, n1):
                        late = int(j < 6)
                        c = o - (OCTETS + 1 + late)
                        if k == 0:
                            dve.wait_ge(s_gate, c + 1)
                        if oc.rep > OCTETS + 1 + late or k >= 2:
                            dve.wait_ge(stored[k % 2], (c * 2 + k // 2) * 16)
                        ch = C // 4
                        V.tensor_tensor(product[k % 2][:, :, :],
                                        x2[:, ds((o + late + 1) % 2, 1), ch * k:ch * (k + 1), :].rearrange("p a c t -> p (a c) t"),
                                        gate[:, :].rearrange("p (a t) -> p a t", a=1).broadcast_to([P, ch, COLS]),
                                        ALU.mult).then_inc(s_product, 1)

            octets(dve, images, body)

        @block.tensor
        def _(pe):
            T = nc.tensor

            def body(oc):
                o = oc.o
                for j in range(STEPS):
                    dec = oc.rep % OCTETS == 0 and OCTETS <= oc.rep <= images * OCTETS
                    if dec and j == TURN_STEP:
                        pe.wait_ge(s_best, o)
                        T.transpose(decode[0:GC, 0:P], best[:, :], ident[:, :]).then_inc(s_bestT, 1)
                    if dec and j == TURN_STEP + 1:
                        pe.wait_ge(s_dec, oc.image * 4)
                        T.matmul(decode[:, P:P + GC], pick[0:GC, 0:P], kval[:, :], start=True, stop=True)\
                            .then_inc(s_spread, 1)
                    if oc.exists(j, SHIFT, n1):
                        e, s = oc.count(j, SHIFT), (j - SHIFT) % STEPS
                        pe.wait_ge(s_floors, e + 1)
                        if oc.at_least(j, SHIFT, 1):
                            pe.wait_ge(s_att, e)
                        q = floors[s % 2][:, :].bitcast(bf16)
                        for k in range(SUB // 2):
                            last = T.transpose(turned[:, P * k:P * (k + 1)], q[:, P * k:P * (k + 1)], ident_bf[:, :])
                        last.then_inc(s_turned, 1)
                    if oc.exists(j, SHIFT + 1, n1):
                        e = oc.count(j, SHIFT + 1)
                        pe.wait_ge(s_att, e + 1)
                        if oc.at_least(j, SHIFT + 1, 1):
                            pe.wait_ge(s_hidden, e)
                        for h in range(2):
                            for n in range(3):
                                last = T.matmul(pre[:, 512 * h:512 * (h + 1)], w_part[n][:, :], att[:, 512 * h:512 * (h + 1)],
                                                start=n == 0, stop=n == 2)
                        last.then_inc(s_conv1, 1)
                    if oc.exists(j, 1, n1):
                        i, b = oc.count(j, 1), (j - 1) % 2
                        pe.wait_ge(s_onehots, i + 1)
                        if oc.at_least(j, 1, 2):
                            pe.wait_ge(s_small, i - 1)
                        pe.sem_inc(hist_begun, 1)
                        oh, ol = onehot_h[b][:, :].bitcast(fp8), onehot_l[b][:, :].bitcast(fp8)
                        for t in range(COLS):
                            k = t // PACK
                            last = T.matmul(counts[b][:, WN * k:WN * (k + 1)], oh[:, WM * t:WM * (t + 1)],
                                            ol[:, WN * t:WN * (t + 1)], start=t % PACK == 0, stop=t % PACK == PACK - 1)
                        last.then_inc(s_hist, 1)
                    if oc.exists(j, 2, n1):
                        i, s = oc.count(j, 2), (j - 2) % STEPS
                        pe.wait_ge(s_small, i + 1)
                        pe.wait_ge(s_big, i + 1)
                        if s == 0 and oc.at_least(j, 2, STEPS):
                            pe.wait_ge(s_key, o * 2)
                        for a, part in ((0, small), (1, big)):
                            for k in range(PARTS):
                                last = T.matmul(totals[:, a, s // 4, :], ident_hf[:, :], part[:, WN * k:WN * (k + 1)],
                                                start=s == 0 and a == 0 and k == 0,
                                                stop=s % 4 == 3 and k == PARTS - 1, skip_group_check=True)
                        last.then_inc(s_totals, 1)
                    if oc.exists(j, SHIFT + 1, n1):
                        e, s = oc.count(j, SHIFT + 1), (j - SHIFT - 1) % STEPS
                        pe.wait_ge(s_hidden, e + 1)
                        if s == 0 and oc.at_least(j, SHIFT + 1, STEPS):
                            pe.wait_ge(s_gate, o - OCTETS)
                        for k in range(SUB // 2):
                            col = SUB * s + 2 * k
                            last = T.matmul(logit[:, col:col + 2], hidden[:, P * k:P * (k + 1)], w2[:, :],
                                            start=True, stop=True)
                        last.then_inc(s_conv2, 1)

            pe.wait_ge(setup_dve, SETUP)
            octets(pe, images, body)


def constants():
    import numpy as np
    ident = np.eye(P, dtype=np.float32)
    m = np.arange(P)
    hi = m // 16 + 8 * (m % 2)
    ch = (m % 16) // 2
    n = np.arange(2 * NL * GC)
    keys = np.zeros((P, 2, 2, 2 * NL * GC), np.float32)
    for a in range(2):
        lo = np.array(LOWS)[n // 16] + 8 * (n % 2) + 2 * a
        same = ch[:, None] == ((n % 16) // 2)[None, :]
        k = (16 * hi[:, None] + lo[None, :]) - (1 << 23)
        keys[:, :, a, :] = np.where(same, k, -(1 << 25))[:, None, :]
    pick = np.zeros((P, P + GC), np.float32)
    for p in range(P):
        pick[(p % C) // GC, p] = 1
        pick[p, P + p % GC] = 1
    return ident, keys.reshape(P, -1), pick


def kernel(**inputs):
    import numpy as np
    import concourse.bacc as bacc
    from concourse.bass_utils import run_bass_kernel_spmd

    x = np.asarray(inputs["x"])
    images = x.shape[0]
    vec = {k.removeprefix("L0_conv_"): np.asarray(v) for k, v in inputs.items() if k != "x"}
    w1t = np.zeros((P, P), np.float32)
    w2b = np.zeros((P, 2), np.float32)
    for h in range(2):
        w1t[C * h:C * (h + 1), C * h:C * (h + 1)] = vec["conv1_w"].T
        w2b[C * h:C * (h + 1), h] = vec["conv2_w"][0]
    par = np.zeros((P, 10), np.float32)
    for k, name in enumerate(("conv1_b", "bn1_gamma", "bn1_beta", "bn1_mean", "bn1_var")):
        par[0:C, k] = vec[name]
        par[C:P, k] = vec[name]
    for k, name in enumerate(("conv2_b", "bn2_gamma", "bn2_beta", "bn2_mean", "bn2_var")):
        par[:, 5 + k] = vec[name][0]
    ident, keys, pick = constants()
    arrays = {"in_x": np.ascontiguousarray(x).reshape(images * C, PIX), "in_w1t": w1t, "in_w2": w2b, "in_par": par,
              "in_ident": ident, "in_keys": keys, "in_pick": pick}
    nc = bacc.Bacc("TRN2", target_bir_lowering=False, num_devices=1)
    aps = [nc.dram_tensor(k, a.shape, mybir.dt.float32, kind="ExternalInput").ap() for k, a in arrays.items()]
    out = nc.dram_tensor("out_y", (images * C, PIX), mybir.dt.float32, kind="ExternalOutput").ap()
    build(nc, *aps, out, float(np.float32(256 / 255.0)))
    r = run_bass_kernel_spmd(nc, [arrays], core_ids=[0])
    return r.results[0]["out_y"].reshape(x.shape)
```
